# Optimizing a Trainium2 kernel written in Bass

```python
import numpy as np
import jax
import jax.numpy as jnp

def _softmax(x, axis=-1):
    return jax.nn.softmax(x, axis=axis)

def _gelu(x):
    return jax.nn.gelu(x, approximate=True)

def _silu(x):
    return jax.nn.silu(x)

def _sigmoid(x):
    return jax.nn.sigmoid(x)

def _layernorm(x, axis=-1, eps=1e-05):
    m = jnp.mean(x, axis=axis, keepdims=True)
    v = jnp.var(x, axis=axis, keepdims=True)
    return (x - m) / jnp.sqrt(v + eps)

def _scatter_add(tgt, idx, src, axis=0):
    return tgt.at[idx].add(src)

def _segment_sum(src, seg, n):
    return jax.ops.segment_sum(src, seg, n)
kernel_name = 'mk_adj_preln_d2_adj_r2_d14703'

def setup_inputs(seed: int=0):
    np.random.seed(seed)
    _w = jnp.asarray

    def _rec_inputs():
        import jax
        import jax.numpy as jnp
        _gk = jax.random.key(seed)
        x = -0.0003929 + 0.9999 * jax.random.normal(jax.random.fold_in(_gk, 1), (16, 512, 256), jnp.float32)
        _w = (1.0 + jnp.arange(512, dtype=jnp.float32)) ** (-0.5)
        _w = _w / _w.mean()
        _pij = jnp.clip(0.03125 * _w[:, None] * _w[None, :], 0.0, 1.0)
        _a = jax.random.uniform(jax.random.fold_in(_gk, 2), (512, 512)) < _pij
        _a = jnp.logical_or(_a, jnp.eye(512, dtype=bool))
        _af = _a.astype(jnp.float32)
        _af = _af * jax.random.uniform(jax.random.fold_in(_gk, 3), (512, 512), jnp.float32, 0.05, 1)
        adj = _af
        return (x, adj)
    x, adj = _rec_inputs()

    def _L0_gnn_setup():
        import jax, jax.numpy as jnp
        import numpy as np
        B, N, D, O = (8, 2048, 256, 256)
        key = jax.random.key(seed)
        k1, k2, k3, k4 = jax.random.split(key, 4)
        x = jax.random.normal(k1, (B, N, D), dtype=jnp.float32)
        adj = jax.random.uniform(k2, (N, N), dtype=jnp.float32)
        weight = jax.random.normal(k3, (D, O), dtype=jnp.float32) * 0.02
        bias = jax.random.normal(k4, (O,), dtype=jnp.float32) * 0.02
        return {'x': x, 'adj': adj, 'weight': weight, 'bias': bias}
    _L0_gnn_all = _L0_gnn_setup()
    _L0_gnn_in = {k: v for k, v in _L0_gnn_all.items() if k in ('weight', 'bias')}
    del _L0_gnn_all

    def _L1_gnn_setup():
        import jax, jax.numpy as jnp
        import numpy as np
        B, N, D, T = (64, 128, 256, 3)

        def _lin(v, W, b):
            return jnp.einsum('...i,oi->...o', v, W) + b
        key = jax.random.key(seed)
        ks = jax.random.split(key, 12)
        s2 = 1.0 / np.sqrt(2 * D)
        s1 = 1.0 / np.sqrt(D)
        return {'x': jax.random.normal(ks[0], (B, N, D), jnp.float32), 'in_mat': jax.random.uniform(ks[1], (N, N), jnp.float32) / N, 'out_mat': jax.random.uniform(ks[2], (N, N), jnp.float32) / N, 'w3_w': jax.random.normal(ks[3], (D, 2 * D), jnp.float32) * s2, 'w3_b': jnp.zeros((D,), jnp.float32), 'u3_w': jax.random.normal(ks[4], (D, D), jnp.float32) * s1, 'u3_b': jnp.zeros((D,), jnp.float32), 'w4_w': jax.random.normal(ks[5], (D, 2 * D), jnp.float32) * s2, 'w4_b': jnp.zeros((D,), jnp.float32), 'w5_w': jax.random.normal(ks[6], (D, 2 * D), jnp.float32) * s2, 'w5_b': jnp.zeros((D,), jnp.float32), 'u5_w': jax.random.normal(ks[7], (D, D), jnp.float32) * s1, 'u5_b': jnp.zeros((D,), jnp.float32)}
    _L1_gnn_all = _L1_gnn_setup()
    _L1_gnn_in = {k: v for k, v in _L1_gnn_all.items() if k in ('w3_w', 'w3_b', 'u3_w', 'u3_b', 'w4_w', 'w4_b', 'w5_w', 'w5_b', 'u5_w', 'u5_b')}
    del _L1_gnn_all
    return {'x': x, 'adj': adj, 'L0_gnn_weight': _L0_gnn_in['weight'], 'L0_gnn_bias': _L0_gnn_in['bias'], 'L1_gnn_w3_w': _L1_gnn_in['w3_w'], 'L1_gnn_w3_b': _L1_gnn_in['w3_b'], 'L1_gnn_u3_w': _L1_gnn_in['u3_w'], 'L1_gnn_u3_b': _L1_gnn_in['u3_b'], 'L1_gnn_w4_w': _L1_gnn_in['w4_w'], 'L1_gnn_w4_b': _L1_gnn_in['w4_b'], 'L1_gnn_w5_w': _L1_gnn_in['w5_w'], 'L1_gnn_w5_b': _L1_gnn_in['w5_b'], 'L1_gnn_u5_w': _L1_gnn_in['u5_w'], 'L1_gnn_u5_b': _L1_gnn_in['u5_b']}

def reference(x, adj, L0_gnn_weight, L0_gnn_bias, L1_gnn_w3_w, L1_gnn_w3_b, L1_gnn_u3_w, L1_gnn_u3_b, L1_gnn_w4_w, L1_gnn_w4_b, L1_gnn_w5_w, L1_gnn_w5_b, L1_gnn_u5_w, L1_gnn_u5_b):
    import jax
    import jax.numpy as jnp

    def _L0_gnn_ref(x, adj, weight, bias):
        import jax, jax.numpy as jnp
        import numpy as np
        B, N, D, O = (8, 2048, 256, 256)
        y = jnp.einsum('nm,bmd->bnd', adj, x)
        out = jnp.einsum('bnd,do->bno', y, weight) + bias
        return out

    def _L1_gnn_ref(x, in_mat, out_mat, w3_w, w3_b, u3_w, u3_b, w4_w, w4_b, w5_w, w5_b, u5_w, u5_b):
        import jax, jax.numpy as jnp
        import numpy as np
        B, N, D, T = (64, 128, 256, 3)

        def _lin(v, W, b):
            return jnp.einsum('...i,oi->...o', v, W) + b
        h = x
        for _ in range(T):
            a_in = jnp.einsum('nm,bmd->bnd', in_mat, h)
            a_out = jnp.einsum('nm,bmd->bnd', out_mat, h)
            av = jnp.concatenate([a_in, a_out], axis=-1)
            z = jax.nn.sigmoid(_lin(av, w3_w, w3_b) + _lin(h, u3_w, u3_b))
            r = jax.nn.sigmoid(_lin(av, w4_w, w4_b) + _lin(h, u3_w, u3_b))
            hv = jnp.tanh(_lin(av, w5_w, w5_b) + _lin(r * h, u5_w, u5_b))
            h = (1.0 - z) * h + z * hv
        return h
    h = jnp.maximum(_layernorm(x, axis=-1), 0.0)
    x = x + _L0_gnn_ref(h, adj, L0_gnn_weight, L0_gnn_bias)
    h = jnp.maximum(_layernorm(x, axis=-1), 0.0)
    x = x + _L1_gnn_ref(h, adj, adj, L1_gnn_w3_w, L1_gnn_w3_b, L1_gnn_u3_w, L1_gnn_u3_b, L1_gnn_w4_w, L1_gnn_w4_b, L1_gnn_w5_w, L1_gnn_w5_b, L1_gnn_u5_w, L1_gnn_u5_b)
    return x

_drawn_inputs = setup_inputs


def setup_inputs(seed=0):
    import zlib

    import numpy as np

    out = dict(_drawn_inputs(seed))
    spreads = {'L1_gnn_w3_b': (0.0, 0.42),
     'L1_gnn_u3_b': (0.0, 0.344),
     'L1_gnn_w4_b': (0.0, 2.0),
     'L1_gnn_w5_b': (0.0, 0.1),
     'L1_gnn_u5_b': (0.0, 0.1)}
    factors = {}
    for name, (base, spread) in spreads.items():
        noise = np.random.default_rng([zlib.crc32(name.encode()), seed]).standard_normal(out[name].shape)
        drawn = base * np.exp(spread * noise) if base else spread * noise
        out[name] = jnp.asarray(drawn.astype(out[name].dtype))
    for name, factor in factors.items():
        out[name] = (out[name] * factor).astype(out[name].dtype)
    return out
```

```python
from contextlib import ExitStack

import concourse.bass as bass
from concourse import mybir

P = 128
F32 = mybir.dt.float32
F32R = mybir.dt.float32r
ALU = mybir.AluOpType
ACT = mybir.ActivationFunctionType
EPS = 1e-5

W3, W4, W5, U3, U5, W0 = range(6)


def adjacency_blocks_kernel(nc, x, adj, l0_weight, l0_bias, w3_w, w3_b, u3_w, u3_b,
                            w4_w, w4_b, w5_w, w5_b, u5_w, u5_b, out):
    B, N, D = x.shape
    T = N // P
    J = D // P
    PAIRS = B // 2
    STEPS = 3
    SLOTS = 2 * STEPS
    LAST = PAIRS - 1
    HALF = T // J
    assert N == 512 and D == 256 and B % 2 == 0

    ADJ = 2 * (2 + SLOTS)
    SLOT = 2 * SLOTS
    TURN = 2 * (2 + SLOTS)
    HSPL = 2 * SLOTS
    NAT = 2 * (2 + SLOTS)
    LN = 4

    ctx = ExitStack()
    with ctx:
        def sb(name, shape, dt=F32):
            return ctx.enter_context(nc.sbuf_tensor(name, shape, dt))

        def sem(name):
            return ctx.enter_context(nc.semaphore(name))

        def banks(name):
            return [ctx.enter_context(nc.psum_tensor(f"{name}{j}", [P, N], F32)) for j in range(J)]

        ps_a = banks("ps_a")
        ps_z = banks("ps_z")
        ps_r = banks("ps_r")
        ps_v = banks("ps_v")

        ident = sb("ident", [P, P])
        adjt_hi = sb("adjt_hi", [P, T, N], F32R)
        adjt_lo = sb("adjt_lo", [P, T, N], F32R)
        w_hi = sb("w_hi", [P, 6, J, D], F32R)
        w_lo = sb("w_lo", [P, 6, J, D], F32R)
        bias_row = sb("bias_row", [P, D])
        w_bias = sb("w_bias", [3 * J, P])
        u_bias = sb("u_bias", [3 * J, P])
        bias_sum = sb("bias_sum", [3 * J, P])
        gate_bias = sb("gate_bias", [P, 3, J])
        minus_half = sb("minus_half", [P, T])
        adj_raw = sb("adj_raw", [P, T, N])
        gate_raw = [sb(f"gate_raw{m}", [P, J, 2 * D]) for m in range(3)]
        gate_sum = [sb(f"gate_sum{m}", [P, J, D]) for m in range(3)]
        u_raw = [sb(f"u_raw{m}", [P, J, D]) for m in range(2)]
        w0_raw = sb("w0_raw", [P, J, D])

        xs = [sb(f"xs{s}", [P, T, D]) for s in range(2)]
        x2 = [sb(f"x2_{s}", [P, T, D]) for s in range(2)]
        nat_hi = [sb(f"nat_hi{s}", [P, T, D], F32R) for s in range(2)]
        nat_lo = [sb(f"nat_lo{s}", [P, T, D], F32R) for s in range(2)]
        h = [sb(f"h{s}", [P, J, N]) for s in range(2)]
        h_hi = [sb(f"h_hi{s}", [P, J, N], F32R) for s in range(2)]
        h_lo = [sb(f"h_lo{s}", [P, J, N], F32R) for s in range(2)]
        a_hi = [sb(f"a_hi{s}", [P, J, N], F32R) for s in range(2)]
        a_lo = [sb(f"a_lo{s}", [P, J, N], F32R) for s in range(2)]
        xn = [sb(f"xn{s}", [P, T, D]) for s in range(2)]
        outs = [sb(f"outs{s}", [P, T, D]) for s in range(2)]
        hu = sb("hu", [P, J, N])
        r = sb("r", [P, J, N])
        z = sb("z", [P, J, N])
        v = sb("v", [P, J, N])
        keep = sb("keep", [P, J, N])
        rh_hi = sb("rh_hi", [P, J, N], F32R)
        rh_lo = sb("rh_lo", [P, J, N], F32R)
        stats = sb("stats", [P, T, 6])
        meanvar = sb("meanvar", [P, T, 2])
        vareps = sb("vareps", [P, T])
        rstd = sb("rstd", [P, T])

        adj_loaded, gates_loaded, small_loaded = sem("adj_loaded"), sem("gates_loaded"), sem("small_loaded")
        x_loaded = [sem(f"x_loaded{s}") for s in range(2)]
        out_stored = [sem(f"out_stored{s}") for s in range(2)]
        zeroed, ident_ready, consts_ready = sem("zeroed"), sem("ident_ready"), sem("consts_ready")
        gate_sums_ready, bias_turned, gate_bias_ready = sem("gate_sums_ready"), sem("bias_turned"), sem("gate_bias_ready")
        setup_turned, setup_hi, setup_lo = sem("setup_turned"), sem("setup_hi"), sem("setup_lo")
        adj_done, hu_done, r_done, z_done, v_done = (sem(f"{k}_done") for k in ("adj", "hu", "r", "z", "v"))
        proj_done, turned = sem("proj_done"), sem("turned")
        a_hi_ready, hu_copied, r_ready = sem("a_hi_ready"), sem("hu_copied"), sem("r_ready")
        rh_hi_ready, z_ready, v_ready = sem("rh_hi_ready"), sem("z_ready"), sem("v_ready")
        h_init, h_hi_ready, nat_hi_ready = sem("h_init"), sem("h_hi_ready"), sem("nat_hi_ready")
        a_lo_ready, r_sum_ready, rh_ready = sem("a_lo_ready"), sem("r_sum_ready"), sem("rh_ready")
        rh_lo_ready, keep_ready, zv_ready = sem("rh_lo_ready"), sem("keep_ready"), sem("zv_ready")
        h_new, h_lo_ready, nat_lo_ready = sem("h_new"), sem("h_lo_ready"), sem("nat_lo_ready")
        var_ready, vareps_ready, xn_ready = (sem(k) for k in ("var_ready", "vareps_ready", "xn_ready"))
        x2_ready, out_ready = sem("x2_ready"), sem("out_ready")
        rstd_ready, xb_ready = sem("rstd_ready"), sem("xb_ready")

        first_bank = (ps_z, ps_r)

        x_rows = x.rearrange("b (p t) d -> b p t d", t=T)
        out_rows = out.rearrange("b (p t) d -> b p t d", t=T)

        ADJ_GROUPS = T
        setup_bank = [ps_z[0], ps_z[1], ps_r[0], ps_r[1], ps_v[0], ps_v[1], ps_r[0], ps_r[1], ps_v[0]]
        setup_before = [None, None, None, None, None, None, 2, 3, 4]
        turned_weight = [W3, W4, W5, U3, U5]

        block = ctx.enter_context(nc.Block())

        @block.sync
        def _(sp):
            sp.dma_start(adj_raw[:], adj.rearrange("(p t) m -> p t m", t=T)).then_inc(adj_loaded, 16)
            for s in range(2):
                sp.dma_start(xs[s][:], x_rows[s]).then_inc(x_loaded[s], 16)
                if s == 0:
                    sp.dma_start(w0_raw[:], l0_weight.rearrange("(k p) o -> p k o", p=P)).then_inc(gates_loaded, 16)
            for raw, w in zip(gate_raw + u_raw, (w3_w, w4_w, w5_w, u3_w, u5_w)):
                sp.dma_start(raw[:], w.rearrange("(j p) i -> p j i", p=P)).then_inc(gates_loaded, 16)

            def pair(n, last):
                if not (isinstance(n, int) and n == 0):
                    for s in range(2):
                        sp.wait_ge(out_stored[s], 16 * n)
                if not last:
                    for s in range(2):
                        sp.wait_ge(x2_ready, 4 * n + 2 * s + 2)
                        sp.dma_start(xs[s][:], x_rows[2 * n + 2 + s]).then_inc(x_loaded[s], 16)
                for s in range(2):
                    sp.wait_ge(out_ready, 4 * n + 2 * s + 2)
                    sp.dma_start(out_rows[2 * n + s], outs[s][:]).then_inc(out_stored[s], 16)

            pair(0, False)
            with sp.Fori(1, LAST) as n:
                pair(n, False)
            pair(LAST, True)
            for s in range(2):
                sp.wait_ge(out_stored[s], 16 * PAIRS)

        @block.gpsimd
        def _(pool):
            pool.dma_start(bias_row[:], l0_bias.partition_broadcast(P)).then_inc(small_loaded, 16)
            for to, vectors in ((w_bias, (w3_b, w4_b, w5_b)), (u_bias, (u3_b, u3_b, u5_b))):
                for m, b in enumerate(vectors):
                    pool.dma_start(to[m * J:(m + 1) * J, :], b.rearrange("(j p) -> j p", p=P)).then_inc(small_loaded, 16)
            pool.memset(ident[:], 0.0).then_inc(zeroed, 1)
            pool.memset(minus_half[:], -0.5).then_inc(consts_ready, 1)
            pool.wait_ge(zeroed, 1)
            pool.affine_select(out=ident[:], in_=ident[:], compare_op=ALU.not_equal, fill=1.0, base=0,
                               pattern=[[-1, P]], channel_multiplier=1).then_inc(ident_ready, 1)

            def inverse_std(n, k):
                pool.wait_ge(vareps_ready, LN * n + k + 1)
                pool.tensor_tensor(rstd[:], vareps[:], minus_half[:], ALU.pow).then_inc(rstd_ready, 1)

            def add_bias(n, s):
                pool.wait_ge(xn_ready, 2 * (LN * n + s) + 2)
                for t in range(T):
                    ins = pool.tensor_tensor(xs[s][:, t, :], xs[s][:, t, :], bias_row[:], ALU.add)
                ins.then_inc(xb_ready, 1)

            pool.wait_ge(consts_ready, 1)
            inverse_std(0, 0)
            pool.wait_ge(small_loaded, 16 * 7)
            add_bias(0, 0)
            pool.wait_ge(gates_loaded, 16 * 6)
            for m in range(3):
                pool.tensor_tensor(gate_sum[m][:], gate_raw[m][:, :, 0:D], gate_raw[m][:, :, D:2 * D],
                                   ALU.add).then_inc(gate_sums_ready, 1)
            pool.tensor_tensor(bias_sum[:], w_bias[:], u_bias[:], ALU.add).then_inc(gate_sums_ready, 1)
            inverse_std(0, 1)
            add_bias(0, 1)
            inverse_std(0, 2)

            def pair(n, last):
                inverse_std(n, 3)
                if not last:
                    for s in range(2):
                        inverse_std(n + 1, s)
                        add_bias(n + 1, s)
                    inverse_std(n + 1, 2)

            with pool.Fori(0, LAST) as n:
                pair(n, False)
            pair(LAST, True)

        @block.tensor
        def _(pe):
            def setup_turn(g):
                if setup_before[g] is not None:
                    pe.wait_ge(setup_lo, setup_before[g] + 1)
                for c in range(4):
                    if g < ADJ_GROUPS:
                        tile = adj_raw[:, c, g:N:T]
                    else:
                        k, j = c // J, c % J
                        tile = (gate_sum + u_raw)[g - ADJ_GROUPS][:, j, k * P:(k + 1) * P]
                    mm = pe.transpose(setup_bank[g][:, c * P:(c + 1) * P], tile, ident[:])
                mm.then_inc(setup_turned, 1)

            def mixed(n, q, s):
                for j in range(J):
                    if not (q == 0 and isinstance(n, int) and n == 0):
                        pe.wait_ge(a_lo_ready, ADJ * n + 2 * (q - 1) + j + 1)
                    for k in range(T):
                        if j == 0 and k % HALF == 0:
                            pe.wait_ge(nat_hi_ready, NAT * n + 2 * q + k // HALF + 1)
                            pe.wait_ge(nat_lo_ready, NAT * n + 2 * q + k // HALF + 1)
                        hi = nat_hi[s][:, k, j * P:(j + 1) * P]
                        lo = nat_lo[s][:, k, j * P:(j + 1) * P]
                        pe.matmul(ps_a[j][:], hi, adjt_hi[:, k, :], start=(k == 0), stop=False)
                        pe.matmul(ps_a[j][:], hi, adjt_lo[:, k, :], start=False, stop=False)
                        mm = pe.matmul(ps_a[j][:], lo, adjt_hi[:, k, :], start=False, stop=(k == T - 1))
                    mm.then_inc(adj_done, 1)

            def weighted(bank, w, j, hi, lo, start, stop):
                for k in range(J):
                    whi = w_hi[:, w, k, j * P:(j + 1) * P]
                    wlo = w_lo[:, w, k, j * P:(j + 1) * P]
                    pe.matmul(bank[:], whi, hi[:, k, :], start=(start and k == 0), stop=False, skip_group_check=True)
                    pe.matmul(bank[:], whi, lo[:, k, :], start=False, stop=False, skip_group_check=True)
                    mm = pe.matmul(bank[:], wlo, hi[:, k, :], start=False, stop=(stop and k == J - 1),
                                   skip_group_check=True)
                return mm

            def project(n, s):
                bank = (ps_z, ps_v)[s]
                if s == 0 and not (isinstance(n, int) and n == 0):
                    pe.wait_ge(z_ready, SLOT * n)
                pe.wait_ge(a_hi_ready, ADJ * n + 2 * s + 2)
                pe.wait_ge(a_lo_ready, ADJ * n + 2 * s + 2)
                for t in range(T):
                    to = bank[t // HALF][:, (t % HALF) * D:(t % HALF + 1) * D]
                    for k in range(J):
                        yhi = a_hi[s][:, k, t * P:(t + 1) * P]
                        ylo = a_lo[s][:, k, t * P:(t + 1) * P]
                        pe.matmul(to, yhi, w_hi[:, W0, k, :], start=(k == 0), stop=False)
                        pe.matmul(to, yhi, w_lo[:, W0, k, :], start=False, stop=False)
                        mm = pe.matmul(to, ylo, w_hi[:, W0, k, :], start=False, stop=(k == J - 1))
                    if t % HALF == HALF - 1:
                        mm.then_inc(proj_done, 1)

            def turn_first(n, s):
                pe.wait_ge(xn_ready, 2 * (LN * n + 2 + s) + 2)
                if s == 1:
                    pe.wait_ge(r_sum_ready, SLOT * n + 2)
                for j in range(J):
                    for t in range(T):
                        mm = pe.transpose(first_bank[s][j][:, t * P:(t + 1) * P], xn[s][:, t, j * P:(j + 1) * P], ident[:])
                    mm.then_inc(turned, 1)

            def turn_back(n, c):
                s = c % 2
                pe.wait_ge(h_new, SLOT * n + 2 * c + 2)
                if c < SLOTS - 1:
                    pe.wait_ge(r_sum_ready, SLOT * n + 2 * (c + 1) + 2)
                else:
                    pe.wait_ge(out_ready, 4 * n + 2)
                for b in range(J):
                    for t in range(HALF):
                        for j in range(J):
                            f = (b * HALF + t) * P
                            mm = pe.transpose(ps_r[b][:, t * D + j * P:t * D + (j + 1) * P],
                                              h[s][:, j, f:f + P], ident[:])
                    mm.then_inc(turned, 1)

            def slot(n, c, last):
                s = c % 2
                mixed(n, 2 + c, s)
                pe.wait_ge(h_hi_ready, HSPL * n + 2 * c + 2)
                pe.wait_ge(h_lo_ready, HSPL * n + 2 * c + 2)
                for j in range(J):
                    if c == 0:
                        pe.wait_ge(h_init, 4 * n + j + 1)
                    else:
                        pe.wait_ge(z_ready, SLOT * n + 2 * (c - 1) + j + 1)
                    weighted(ps_z[j], U3, j, h_hi[s], h_lo[s], True, True).then_inc(hu_done, 1)
                pe.wait_ge(a_hi_ready, ADJ * n + 2 * (2 + c) + 2)
                pe.wait_ge(a_lo_ready, ADJ * n + 2 * (2 + c) + 2)
                for j in range(J):
                    if c == 1:
                        pe.wait_ge(h_init, 4 * n + 2 * c + j + 1)
                    elif c > 1:
                        pe.wait_ge(nat_lo_ready, NAT * n + 2 * (c + 2) + j + 1)
                    weighted(ps_r[j], W4, j, a_hi[s], a_lo[s], True, True).then_inc(r_done, 1)
                for j in range(J):
                    pe.wait_ge(hu_copied, SLOT * n + 2 * c + j + 1)
                    weighted(ps_z[j], W3, j, a_hi[s], a_lo[s], False, True).then_inc(z_done, 1)
                if c == SLOTS - 1 and not last:
                    mixed(n + 1, 0, 0)
                for j in range(J):
                    if c == 0:
                        pe.wait_ge(x2_ready, 4 * n + 2 + j + 1)
                    else:
                        pe.wait_ge(v_ready, SLOT * n + 2 * (c - 1) + j + 1)
                    weighted(ps_v[j], W5, j, a_hi[s], a_lo[s], True, False)
                if c == 0:
                    turn_first(n, 1)
                else:
                    turn_back(n, c - 1)
                pe.wait_ge(rh_hi_ready, SLOT * n + 2 * c + 2)
                pe.wait_ge(rh_lo_ready, SLOT * n + 2 * c + 2)
                for j in range(J):
                    weighted(ps_v[j], U5, j, rh_hi, rh_lo, False, True).then_inc(v_done, 1)

            pe.wait_ge(ident_ready, 1)
            pe.wait_ge(adj_loaded, 16)
            for g in range(ADJ_GROUPS):
                setup_turn(g)
            pe.wait_ge(setup_hi, ADJ_GROUPS)
            pe.wait_ge(setup_lo, ADJ_GROUPS)
            mixed(0, 0, 0)
            pe.wait_ge(gates_loaded, 16 * 6)
            pe.wait_ge(gate_sums_ready, 4)
            for g in range(ADJ_GROUPS, len(setup_bank)):
                setup_turn(g)
            pe.wait_ge(setup_lo, 6)
            pe.transpose(ps_v[1][:, 0:3 * J], bias_sum[:], ident[0:3 * J, 0:3 * J]).then_inc(bias_turned, 1)
            pe.wait_ge(setup_hi, len(setup_bank) + 1)
            pe.wait_ge(setup_lo, len(setup_bank) + 1)
            pe.wait_ge(gate_bias_ready, 1)
            project(0, 0)
            mixed(0, 1, 1)

            def pair(n, last):
                turn_first(n, 0)
                project(n, 1)
                for c in range(SLOTS):
                    slot(n, c, last)
                if not last:
                    project(n + 1, 0)
                    mixed(n + 1, 1, 1)
                turn_back(n, SLOTS - 1)

            with pe.Fori(0, LAST) as n:
                pair(n, False)
            pair(LAST, True)

        @block.scalar
        def _(act):
            def copy_setup(g):
                act.wait_ge(setup_turned, g + 1)
                if g < ADJ_GROUPS:
                    to = adjt_hi[:, g, :]
                    act.activation(to, setup_bank[g][:], ACT.Copy).then_inc(setup_hi, 1)
                else:
                    to = w_hi[:, turned_weight[g - ADJ_GROUPS]]
                    act.activation(to, setup_bank[g][:].rearrange("p (k o) -> p k o", k=J),
                                   ACT.Copy).then_inc(setup_hi, 1)

            def split_norm(n, k):
                s = k % 2
                for b in range(J):
                    rows = slice(b * HALF, (b + 1) * HALF)
                    act.wait_ge(xn_ready, 2 * (LN * n + k) + b + 1)
                    act.activation(nat_hi[s][:, rows, :], xn[s][:, rows, :], ACT.Relu).then_inc(nat_hi_ready, 1)

            def split_mixed(n, q, s):
                for j in range(J):
                    act.wait_ge(adj_done, ADJ * n + 2 * q + j + 1)
                    act.activation(a_hi[s][:, j, :], ps_a[j][:], ACT.Copy).then_inc(a_hi_ready, 1)

            def first_state(n, s):
                for j in range(J):
                    act.wait_ge(turned, TURN * n + 2 * s + j + 1)
                    act.activation(h[s][:, j, :], first_bank[s][j][:], ACT.Relu).then_inc(h_init, 1)
                for j in range(J):
                    act.wait_ge(h_init, 4 * n + 2 * s + j + 1)
                    act.activation(h_hi[s][:, j, :], h[s][:, j, :], ACT.Copy).then_inc(h_hi_ready, 1)

            def turned_state(n, c):
                s = c % 2
                for b in range(J):
                    act.wait_ge(turned, TURN * n + 2 * (c + 2) + b + 1)
                    act.activation(nat_hi[s][:, b * HALF:(b + 1) * HALF, :],
                                   ps_r[b][:].rearrange("p (t d) -> p t d", d=D), ACT.Copy).then_inc(nat_hi_ready, 1)

            def slot(n, c, last):
                s = c % 2
                split_mixed(n, 2 + c, s)
                if c == 0:
                    split_norm(n, 3)
                if c == SLOTS - 1 and not last:
                    split_norm(n + 1, 0)
                for j in range(J):
                    act.wait_ge(hu_done, SLOT * n + 2 * c + j + 1)
                    act.activation(hu[:, j, :], ps_z[j][:], ACT.Copy).then_inc(hu_copied, 1)
                for j in range(J):
                    act.wait_ge(r_sum_ready, SLOT * n + 2 * c + j + 1)
                    act.activation(r[:, j, :], r[:, j, :], ACT.Sigmoid,
                                   bias=gate_bias[:, 1, j:j + 1]).then_inc(r_ready, 1)
                for j in range(J):
                    act.wait_ge(rh_ready, SLOT * n + 2 * c + j + 1)
                    act.activation(rh_hi[:, j, :], r[:, j, :], ACT.Copy).then_inc(rh_hi_ready, 1)
                for j in range(J):
                    act.wait_ge(z_done, SLOT * n + 2 * c + j + 1)
                    act.activation(z[:, j, :], ps_z[j][:], ACT.Sigmoid,
                                   bias=gate_bias[:, 0, j:j + 1]).then_inc(z_ready, 1)
                if c == SLOTS - 1 and not last:
                    split_mixed(n + 1, 0, 0)
                    split_norm(n + 1, 1)
                if c == 0:
                    first_state(n, 1)
                elif c < SLOTS - 1:
                    turned_state(n, c - 1)
                for j in range(J):
                    act.wait_ge(v_done, SLOT * n + 2 * c + j + 1)
                    act.activation(v[:, j, :], ps_v[j][:], ACT.Tanh,
                                   bias=gate_bias[:, 2, j:j + 1]).then_inc(v_ready, 1)
                if c < SLOTS - 2:
                    for j in range(J):
                        act.wait_ge(h_new, SLOT * n + 2 * c + j + 1)
                        act.activation(h_hi[s][:, j, :], h[s][:, j, :], ACT.Copy).then_inc(h_hi_ready, 1)

            for g in range(ADJ_GROUPS):
                copy_setup(g)
            split_norm(0, 0)
            split_mixed(0, 0, 0)
            for g in range(ADJ_GROUPS, len(setup_bank)):
                copy_setup(g)
            act.wait_ge(bias_turned, 1)
            act.activation(gate_bias[:], ps_v[1][:, 0:3 * J].rearrange("p (m j) -> p m j", j=J),
                           ACT.Copy).then_inc(gate_bias_ready, 1)
            act.wait_ge(gates_loaded, 16 * 6)
            act.activation(w_hi[:, W0], w0_raw[:], ACT.Copy).then_inc(setup_hi, 1)
            split_norm(0, 1)
            act.wait_ge(gate_bias_ready, 1)
            split_mixed(0, 1, 1)
            split_norm(0, 2)

            def pair(n, last):
                first_state(n, 0)
                for c in range(SLOTS):
                    slot(n, c, last)
                if not last:
                    split_mixed(n + 1, 1, 1)
                    split_norm(n + 1, 2)

            with act.Fori(0, LAST) as n:
                pair(n, False)
            pair(LAST, True)

        @block.vector
        def _(dve):
            def copy_setup(g):
                dve.wait_ge(setup_hi, g + 1)
                if g < ADJ_GROUPS:
                    dve.tensor_tensor(adjt_lo[:, g, :], setup_bank[g][:], adjt_hi[:, g, :].bitcast(F32),
                                      ALU.subtract).then_inc(setup_lo, 1)
                else:
                    m = turned_weight[g - ADJ_GROUPS]
                    dve.tensor_tensor(w_lo[:, m], setup_bank[g][:].rearrange("p (k o) -> p k o", k=J),
                                      w_hi[:, m].bitcast(F32), ALU.subtract).then_inc(setup_lo, 1)

            def norm_stats(n, k, src):
                for t in range(T):
                    dve.bn_stats(stats[:, t, :], src[:, t, :])
                dve.drain()
                for t in range(T):
                    ins = dve.bn_aggr(meanvar[:, t, :], stats[:, t, :])
                ins.then_inc(var_ready, 1)
                dve.wait_ge(var_ready, LN * n + k + 1)
                dve.tensor_scalar(vareps[:], meanvar[:, :, 1], EPS, None, ALU.add).then_inc(vareps_ready, 1)

            def norm_rows(n, k, src):
                s = k % 2
                dve.wait_ge(rstd_ready, LN * n + k + 1)
                for t in range(T):
                    ins = dve.tensor_scalar(xn[s][:, t, :], src[:, t, :], meanvar[:, t, 0:1], rstd[:, t:t + 1],
                                            ALU.subtract, ALU.mult)
                    if t % HALF == HALF - 1:
                        ins.then_inc(xn_ready, 1)

            def norm_split(n, k):
                s = k % 2
                for b in range(J):
                    rows = slice(b * HALF, (b + 1) * HALF)
                    dve.wait_ge(nat_hi_ready, NAT * n + 2 * k + b + 1)
                    dve.scalar_tensor_tensor(out=nat_lo[s][:, rows, :], in0=xn[s][:, rows, :], scalar=0.0,
                                             in1=nat_hi[s][:, rows, :].bitcast(F32), op0=ALU.max,
                                             op1=ALU.subtract).then_inc(nat_lo_ready, 1)

            def first_stats(n, s):
                dve.wait_ge(x_loaded[s], 16 * n + 16)
                norm_stats(n, s, xs[s])

            def split_mixed(n, q, s, tiles=range(J)):
                for j in tiles:
                    dve.wait_ge(a_hi_ready, ADJ * n + 2 * q + j + 1)
                    dve.tensor_tensor(a_lo[s][:, j, :], ps_a[j][:], a_hi[s][:, j, :].bitcast(F32),
                                      ALU.subtract).then_inc(a_lo_ready, 1)

            def residual(n, s):
                dve.wait_ge(xb_ready, 2 * n + s + 1)
                bank = (ps_z, ps_v)[s]
                for b in range(J):
                    rows = slice(b * HALF, (b + 1) * HALF)
                    dve.wait_ge(proj_done, 4 * n + 2 * s + b + 1)
                    dve.tensor_tensor(x2[s][:, rows, :], bank[b][:].rearrange("p (t d) -> p t d", d=D),
                                      xs[s][:, rows, :], ALU.add).then_inc(x2_ready, 1)
                dve.wait_ge(x2_ready, 4 * n + 2 * s + 2)
                norm_stats(n, 2 + s, x2[s])

            def split_state(n, s, q):
                for j in range(J):
                    dve.wait_ge(h_hi_ready, HSPL * n + 2 * q + j + 1)
                    dve.tensor_tensor(h_lo[s][:, j, :], h[s][:, j, :], h_hi[s][:, j, :].bitcast(F32),
                                      ALU.subtract).then_inc(h_lo_ready, 1)

            def turned_state(n, c):
                s = c % 2
                for b in range(J):
                    rows = slice(b * HALF, (b + 1) * HALF)
                    dve.wait_ge(nat_hi_ready, NAT * n + 2 * (c + 4) + b + 1)
                    dve.tensor_tensor(nat_lo[s][:, rows, :], ps_r[b][:].rearrange("p (t d) -> p t d", d=D),
                                      nat_hi[s][:, rows, :].bitcast(F32), ALU.subtract).then_inc(nat_lo_ready, 1)

            def output(n, s):
                if isinstance(n, int) and n > 0:
                    dve.wait_ge(out_stored[s], 16 * n)
                for b in range(J):
                    rows = slice(b * HALF, (b + 1) * HALF)
                    dve.wait_ge(turned, TURN * n + 2 * (SLOTS + s) + b + 1)
                    dve.tensor_tensor(outs[s][:, rows, :], ps_r[b][:].rearrange("p (t d) -> p t d", d=D),
                                      x2[s][:, rows, :], ALU.add).then_inc(out_ready, 1)

            def slot(n, c, last):
                s = c % 2
                if c == 0:
                    split_mixed(n, 2 + c, s, [0])
                    norm_rows(n, 3, x2[1])
                    split_mixed(n, 2 + c, s, [1])
                    norm_split(n, 3)
                else:
                    split_mixed(n, 2 + c, s)
                if c == SLOTS - 1 and not last:
                    norm_rows(n + 1, 0, xs[0])
                    norm_split(n + 1, 0)
                for j in range(J):
                    dve.wait_ge(hu_copied, SLOT * n + 2 * c + j + 1)
                    dve.wait_ge(r_done, SLOT * n + 2 * c + j + 1)
                    dve.tensor_tensor(r[:, j, :], ps_r[j][:], hu[:, j, :], ALU.add).then_inc(r_sum_ready, 1)
                for j in range(J):
                    dve.wait_ge(r_ready, SLOT * n + 2 * c + j + 1)
                    dve.tensor_tensor(r[:, j, :], r[:, j, :], h[s][:, j, :], ALU.mult).then_inc(rh_ready, 1)
                for j in range(J):
                    dve.wait_ge(rh_hi_ready, SLOT * n + 2 * c + j + 1)
                    dve.tensor_tensor(rh_lo[:, j, :], r[:, j, :], rh_hi[:, j, :].bitcast(F32),
                                      ALU.subtract).then_inc(rh_lo_ready, 1)
                for j in range(J):
                    dve.wait_ge(z_ready, SLOT * n + 2 * c + j + 1)
                    dve.scalar_tensor_tensor(out=keep[:, j, :], in0=z[:, j, :], scalar=1.0, in1=h[s][:, j, :],
                                             op0=ALU.subtract, op1=ALU.mult).then_inc(keep_ready, 1)
                if c == SLOTS - 2 and not last:
                    first_stats(n + 1, 0)
                if c == SLOTS - 1 and not last:
                    first_stats(n + 1, 1)
                    split_mixed(n + 1, 0, 0)
                    norm_rows(n + 1, 1, xs[1])
                    norm_split(n + 1, 1)
                if c == 0:
                    split_state(n, 1, 1)
                elif c < SLOTS - 1:
                    turned_state(n, c - 1)
                else:
                    output(n, 0)
                for j in range(J):
                    dve.wait_ge(v_ready, SLOT * n + 2 * c + j + 1)
                    dve.tensor_tensor(v[:, j, :], v[:, j, :], z[:, j, :], ALU.mult).then_inc(zv_ready, 1)
                    dve.wait_ge(zv_ready, SLOT * n + 2 * c + j + 1)
                    dve.wait_ge(keep_ready, SLOT * n + 2 * c + j + 1)
                    dve.tensor_tensor(h[s][:, j, :], v[:, j, :], keep[:, j, :], ALU.subtract).then_inc(h_new, 1)
                if c < SLOTS - 2:
                    split_state(n, s, c + 2)

            def second_norm(n):
                residual(n, 0)
                split_mixed(n, 1, 1, [0])
                norm_rows(n, 2, x2[0])
                split_mixed(n, 1, 1, [1])
                norm_split(n, 2)

            for g in range(ADJ_GROUPS):
                copy_setup(g)
            first_stats(0, 0)
            norm_rows(0, 0, xs[0])
            norm_split(0, 0)
            split_mixed(0, 0, 0)
            for g in range(ADJ_GROUPS, len(setup_bank)):
                copy_setup(g)
            dve.wait_ge(setup_hi, len(setup_bank) + 1)
            dve.tensor_tensor(w_lo[:, W0], w0_raw[:], w_hi[:, W0].bitcast(F32), ALU.subtract).then_inc(setup_lo, 1)
            first_stats(0, 1)
            norm_rows(0, 1, xs[1])
            norm_split(0, 1)
            second_norm(0)

            def pair(n, last):
                split_state(n, 0, 0)
                residual(n, 1)
                for c in range(SLOTS):
                    slot(n, c, last)
                if not last:
                    second_norm(n + 1)
                output(n, 1)
                dve.wait_ge(out_ready, 4 * n + 4)

            with dve.Fori(0, LAST) as n:
                pair(n, False)
            pair(LAST, True)


_INS = ["x", "adj", "L0_gnn_weight", "L0_gnn_bias", "L1_gnn_w3_w", "L1_gnn_w3_b", "L1_gnn_u3_w", "L1_gnn_u3_b",
        "L1_gnn_w4_w", "L1_gnn_w4_b", "L1_gnn_w5_w", "L1_gnn_w5_b", "L1_gnn_u5_w", "L1_gnn_u5_b"]


def kernel(**inputs):
    import numpy as _np
    import concourse.bacc as _bacc
    from concourse import mybir as _mybir
    from concourse.bass_utils import run_bass_kernel_spmd as _run

    nc = _bacc.Bacc("TRN2", target_bir_lowering=False, num_devices=1)
    arrays, args = {}, []
    for name in _INS:
        a = _np.ascontiguousarray(inputs[name])
        arrays[f"in_{name}_dram"] = a
        args.append(nc.dram_tensor(f"in_{name}_dram", a.shape, _mybir.dt.from_np(a.dtype), kind="ExternalInput").ap())
    shape = inputs["x"].shape
    args.append(nc.dram_tensor("out_0_dram", shape, _mybir.dt.float32, kind="ExternalOutput").ap())
    adjacency_blocks_kernel(nc, *args)
    result = _run(nc, [arrays], core_ids=[0])
    return result.results[0]["out_0_dram"]
```

```python
from contextlib import ExitStack

import concourse.bass as bass
from concourse import mybir

P = 128
F32 = mybir.dt.float32
F32R = mybir.dt.float32r
ALU = mybir.AluOpType
ACT = mybir.ActivationFunctionType
EPS = 1e-5

W3, W4, W5, U3, U5, W0 = range(6)


def adjacency_blocks_kernel(nc, x, adj, l0_weight, l0_bias, w3_w, w3_b, u3_w, u3_b,
                            w4_w, w4_b, w5_w, w5_b, u5_w, u5_b, out):
    B, N, D = x.shape
    T = N // P
    J = D // P
    PAIRS = B // 2
    STEPS = 3
    SLOTS = 2 * STEPS
    LAST = PAIRS - 1
    HALF = T // J
    assert N == 512 and D == 256 and B % 2 == 0

    ADJ = 2 * (2 + SLOTS)
    SLOT = 2 * SLOTS
    TURN = 2 * (2 + SLOTS)
    HSPL = 2 * SLOTS
    NAT = 2 * (2 + SLOTS)
    LN = 4

    ctx = ExitStack()
    with ctx:
        def sb(name, shape, dt=F32):
            return ctx.enter_context(nc.sbuf_tensor(name, shape, dt))

        def sem(name):
            return ctx.enter_context(nc.semaphore(name))

        def banks(name):
            return [ctx.enter_context(nc.psum_tensor(f"{name}{j}", [P, N], F32)) for j in range(J)]

        ps_a = banks("ps_a")
        ps_z = banks("ps_z")
        ps_r = banks("ps_r")
        ps_v = banks("ps_v")

        ident = sb("ident", [P, P])
        adjt_hi = sb("adjt_hi", [P, T, N], F32R)
        adjt_lo = sb("adjt_lo", [P, T, N], F32R)
        w_hi = sb("w_hi", [P, 6, J, D], F32R)
        w_lo = sb("w_lo", [P, 6, J, D], F32R)
        bias_row = sb("bias_row", [P, D])
        w_bias = sb("w_bias", [3 * J, P])
        u_bias = sb("u_bias", [3 * J, P])
        bias_sum = sb("bias_sum", [3 * J, P])
        gate_bias = sb("gate_bias", [P, 3, J])
        minus_half = sb("minus_half", [P, T])
        adj_raw = sb("adj_raw", [P, T, N])
        gate_raw = [sb(f"gate_raw{m}", [P, J, 2 * D]) for m in range(3)]
        gate_sum = [sb(f"gate_sum{m}", [P, J, D]) for m in range(3)]
        u_raw = [sb(f"u_raw{m}", [P, J, D]) for m in range(2)]
        w0_raw = sb("w0_raw", [P, J, D])

        xs = [sb(f"xs{s}", [P, T, D]) for s in range(2)]
        x2 = [sb(f"x2_{s}", [P, T, D]) for s in range(2)]
        nat_hi = [sb(f"nat_hi{s}", [P, T, D], F32R) for s in range(2)]
        nat_lo = [sb(f"nat_lo{s}", [P, T, D], F32R) for s in range(2)]
        h = [sb(f"h{s}", [P, J, N]) for s in range(2)]
        h_hi = [sb(f"h_hi{s}", [P, J, N], F32R) for s in range(2)]
        h_lo = [sb(f"h_lo{s}", [P, J, N], F32R) for s in range(2)]
        a_hi = [sb(f"a_hi{s}", [P, J, N], F32R) for s in range(2)]
        a_lo = [sb(f"a_lo{s}", [P, J, N], F32R) for s in range(2)]
        xn = [sb(f"xn{s}", [P, T, D]) for s in range(2)]
        outs = [sb(f"outs{s}", [P, T, D]) for s in range(2)]
        hu = sb("hu", [P, J, N])
        r = sb("r", [P, J, N])
        z = sb("z", [P, J, N])
        v = sb("v", [P, J, N])
        keep = sb("keep", [P, J, N])
        rh_hi = sb("rh_hi", [P, J, N], F32R)
        rh_lo = sb("rh_lo", [P, J, N], F32R)
        stats = sb("stats", [P, T, 6])
        meanvar = sb("meanvar", [P, T, 2])
        vareps = sb("vareps", [P, T])
        rstd = sb("rstd", [P, T])
        table_probe = sb("table_probe", [P, 1])

        adj_loaded = [sem(f"adj_loaded{c}") for c in range(T)]
        gate_loaded = [sem(f"gate_loaded{m}") for m in range(5)]
        w0_loaded, small_loaded = sem("w0_loaded"), sem("small_loaded")
        x_loaded = [sem(f"x_loaded{s}") for s in range(2)]
        out_stored = [sem(f"out_stored{s}") for s in range(2)]
        zeroed, ident_ready, consts_ready = sem("zeroed"), sem("ident_ready"), sem("consts_ready")
        gate_sums_ready, bias_turned, gate_bias_ready = sem("gate_sums_ready"), sem("bias_turned"), sem("gate_bias_ready")
        setup_turned, setup_hi, setup_lo = sem("setup_turned"), sem("setup_hi"), sem("setup_lo")
        adj_done, hu_done, r_done, z_done, v_done = (sem(f"{k}_done") for k in ("adj", "hu", "r", "z", "v"))
        proj_done, turned = sem("proj_done"), sem("turned")
        a_hi_ready, hu_copied, r_ready = sem("a_hi_ready"), sem("hu_copied"), sem("r_ready")
        rh_hi_ready, z_ready, v_ready = sem("rh_hi_ready"), sem("z_ready"), sem("v_ready")
        h_init, h_hi_ready, nat_hi_ready = sem("h_init"), sem("h_hi_ready"), sem("nat_hi_ready")
        a_lo_ready, r_sum_ready, rh_ready = sem("a_lo_ready"), sem("r_sum_ready"), sem("rh_ready")
        rh_lo_ready, keep_ready, zv_ready = sem("rh_lo_ready"), sem("keep_ready"), sem("zv_ready")
        h_new, h_lo_ready, nat_lo_ready = sem("h_new"), sem("h_lo_ready"), sem("nat_lo_ready")
        var_ready, vareps_ready, xn_ready = (sem(k) for k in ("var_ready", "vareps_ready", "xn_ready"))
        x2_ready, out_ready = sem("x2_ready"), sem("out_ready")
        rstd_ready, xb_ready = sem("rstd_ready"), sem("xb_ready")

        first_bank = (ps_z, ps_r)

        x_rows = x.rearrange("b (p t) d -> b p t d", t=T)
        out_rows = out.rearrange("b (p t) d -> b p t d", t=T)

        adj_bank = [ps_v[0], ps_v[1], ps_r[0], ps_r[1]]
        turned_weight = [W3, W4, W5, U3, U5]
        weight_bank = adj_bank + [ps_v[0]]
        WARM_TURNS = 8
        SPLIT_W0 = T
        SPLITS = T + 1 + len(turned_weight)

        first_bank = (ps_z, ps_r)

        x_rows = x.rearrange("b (p t) d -> b p t d", t=T)
        out_rows = out.rearrange("b (p t) d -> b p t d", t=T)

        block = ctx.enter_context(nc.Block())

        @block.sync
        def _(sp):
            sp.dma_start(xs[0][:], x_rows[0]).then_inc(x_loaded[0], 16)
            adj_rows = adj.rearrange("(p t) m -> p t m", t=T)
            for c in range(T):
                sp.dma_start(adj_raw[:, c, :], adj_rows[:, c, :]).then_inc(adj_loaded[c], 16)
            sp.dma_start(w0_raw[:], l0_weight.rearrange("(k p) o -> p k o", p=P)).then_inc(w0_loaded, 16)
            sp.dma_start(xs[1][:], x_rows[1]).then_inc(x_loaded[1], 16)
            for m, w in enumerate((w3_w, w4_w, w5_w, u3_w, u5_w)):
                sp.dma_start((gate_raw + u_raw)[m][:], w.rearrange("(j p) i -> p j i", p=P)).then_inc(gate_loaded[m], 16)
            sp.dma_start(bias_row[:], l0_bias.partition_broadcast(P)).then_inc(small_loaded, 16)
            for to, vectors in ((w_bias, (w3_b, w4_b, w5_b)), (u_bias, (u3_b, u3_b, u5_b))):
                for m, b in enumerate(vectors):
                    sp.dma_start(to[m * J:(m + 1) * J, :], b.rearrange("(j p) -> j p", p=P)).then_inc(small_loaded, 16)

            def pair(n, last):
                if not (isinstance(n, int) and n == 0):
                    for s in range(2):
                        sp.wait_ge(out_stored[s], 16 * J * n)
                if not last:
                    for s in range(2):
                        sp.wait_ge(x2_ready, 4 * n + 2 * s + 2)
                        sp.dma_start(xs[s][:], x_rows[2 * n + 2 + s]).then_inc(x_loaded[s], 16)
                for s in range(2):
                    for b in range(J):
                        rows = slice(b * HALF, (b + 1) * HALF)
                        sp.wait_ge(out_ready, 4 * n + 2 * s + b + 1)
                        sp.dma_start(out_rows[2 * n + s, :, rows, :], outs[s][:, rows, :]).then_inc(out_stored[s], 16)

            pair(0, False)
            with sp.Fori(1, LAST) as n:
                pair(n, False)
            pair(LAST, True)
            for s in range(2):
                sp.wait_ge(out_stored[s], 16 * J * PAIRS)

        @block.gpsimd
        def _(pool):
            pool.memset(ident[:], 0.0).then_inc(zeroed, 1)
            pool.memset(minus_half[:], -0.5).then_inc(consts_ready, 1)
            pool.wait_ge(zeroed, 1)
            pool.affine_select(out=ident[:], in_=ident[:], compare_op=ALU.not_equal, fill=1.0, base=0,
                               pattern=[[-1, P]], channel_multiplier=1).then_inc(ident_ready, 1)

            def inverse_std(n, k):
                pool.wait_ge(vareps_ready, LN * n + k + 1)
                pool.tensor_tensor(rstd[:], vareps[:], minus_half[:], ALU.pow).then_inc(rstd_ready, 1)

            def add_bias(n, s):
                pool.wait_ge(xn_ready, 2 * (LN * n + s) + 2)
                for t in range(T):
                    ins = pool.tensor_tensor(xs[s][:, t, :], xs[s][:, t, :], bias_row[:], ALU.add)
                ins.then_inc(xb_ready, 1)

            pool.wait_ge(consts_ready, 1)
            inverse_std(0, 0)
            for m in range(3):
                if m == 2:
                    inverse_std(0, 1)
                pool.wait_ge(gate_loaded[m], 16)
                pool.tensor_tensor(gate_sum[m][:], gate_raw[m][:, :, 0:D], gate_raw[m][:, :, D:2 * D],
                                   ALU.add).then_inc(gate_sums_ready, 1)
            pool.wait_ge(small_loaded, 16 * 7)
            pool.tensor_tensor(bias_sum[:], w_bias[:], u_bias[:], ALU.add).then_inc(gate_sums_ready, 1)
            add_bias(0, 0)
            add_bias(0, 1)
            inverse_std(0, 2)

            def pair(n, last):
                inverse_std(n, 3)
                if not last:
                    for s in range(2):
                        inverse_std(n + 1, s)
                        add_bias(n + 1, s)
                    inverse_std(n + 1, 2)

            with pool.Fori(0, LAST) as n:
                pair(n, False)
            pair(LAST, True)

        @block.tensor
        def _(pe):
            def turn_adj(c):
                pe.wait_ge(adj_loaded[c], 16)
                for g in range(T):
                    mm = pe.transpose(adj_bank[c][:, g * P:(g + 1) * P], adj_raw[:, c, g:N:T], ident[:])
                mm.then_inc(setup_turned, 1)

            def turn_weight(m):
                if m < 3:
                    pe.wait_ge(gate_sums_ready, m + 1)
                else:
                    pe.wait_ge(gate_loaded[m], 16)
                pe.wait_ge(setup_lo, m + 1 if m < T else SPLIT_W0 + 2)
                for k in range(J):
                    for j in range(J):
                        mm = pe.transpose(weight_bank[m][:, k * D + j * P:k * D + (j + 1) * P],
                                          (gate_sum + u_raw)[m][:, j, k * P:(k + 1) * P], ident[:])
                mm.then_inc(setup_turned, 1)

            def mixed(n, q, s):
                first = q == 0 and isinstance(n, int) and n == 0
                for j in range(J):
                    if not first:
                        pe.wait_ge(a_lo_ready, ADJ * n + 2 * (q - 1) + j + 1)
                    passes = ((nat_hi, adjt_hi), (nat_lo, adjt_hi), (nat_hi, adjt_lo))
                    for i, (rows, columns) in enumerate(passes):
                        if first and j == 0:
                            if i == 0:
                                pe.wait_ge(setup_hi, T)
                            if i == 2:
                                pe.wait_ge(setup_lo, T)
                        for k in range(T):
                            if j == 0 and i < 2 and k % HALF == 0:
                                pe.wait_ge((nat_hi_ready, nat_lo_ready)[i], NAT * n + 2 * q + k // HALF + 1)
                            mm = pe.matmul(ps_a[j][:], rows[s][:, k, j * P:(j + 1) * P], columns[:, k, :],
                                           start=(i == 0 and k == 0), stop=(i == 2 and k == T - 1))
                    mm.then_inc(adj_done, 1)

            def weighted(bank, w, j, hi, lo, start, stop):
                for k in range(J):
                    whi = w_hi[:, w, k, j * P:(j + 1) * P]
                    wlo = w_lo[:, w, k, j * P:(j + 1) * P]
                    pe.matmul(bank[:], whi, hi[:, k, :], start=(start and k == 0), stop=False, skip_group_check=True)
                    pe.matmul(bank[:], whi, lo[:, k, :], start=False, stop=False, skip_group_check=True)
                    mm = pe.matmul(bank[:], wlo, hi[:, k, :], start=False, stop=(stop and k == J - 1),
                                   skip_group_check=True)
                return mm

            def project(n, s):
                bank = (ps_z, ps_v)[s]
                if s == 0 and not (isinstance(n, int) and n == 0):
                    pe.wait_ge(z_ready, SLOT * n)
                pe.wait_ge(a_hi_ready, ADJ * n + 2 * s + 2)
                pe.wait_ge(a_lo_ready, ADJ * n + 2 * s + 2)
                for t in range(T):
                    to = bank[t // HALF][:, (t % HALF) * D:(t % HALF + 1) * D]
                    for k in range(J):
                        yhi = a_hi[s][:, k, t * P:(t + 1) * P]
                        ylo = a_lo[s][:, k, t * P:(t + 1) * P]
                        pe.matmul(to, yhi, w_hi[:, W0, k, :], start=(k == 0), stop=False)
                        pe.matmul(to, yhi, w_lo[:, W0, k, :], start=False, stop=False)
                        mm = pe.matmul(to, ylo, w_hi[:, W0, k, :], start=False, stop=(k == J - 1))
                    if t % HALF == HALF - 1:
                        mm.then_inc(proj_done, 1)

            def turn_first(n, s):
                pe.wait_ge(xn_ready, 2 * (LN * n + 2 + s) + 2)
                if s == 1:
                    pe.wait_ge(r_sum_ready, SLOT * n + 2)
                for j in range(J):
                    for t in range(T):
                        mm = pe.transpose(first_bank[s][j][:, t * P:(t + 1) * P], xn[s][:, t, j * P:(j + 1) * P], ident[:])
                    mm.then_inc(turned, 1)

            def turn_back(n, c):
                s = c % 2
                pe.wait_ge(h_new, SLOT * n + 2 * c + 2)
                if c < SLOTS - 1:
                    pe.wait_ge(r_sum_ready, SLOT * n + 2 * (c + 1) + 2)
                else:
                    pe.wait_ge(out_ready, 4 * n + 2)
                for b in range(J):
                    for t in range(HALF):
                        for j in range(J):
                            f = (b * HALF + t) * P
                            mm = pe.transpose(ps_r[b][:, t * D + j * P:t * D + (j + 1) * P],
                                              h[s][:, j, f:f + P], ident[:])
                    mm.then_inc(turned, 1)

            def slot(n, c, last):
                s = c % 2
                mixed(n, 2 + c, s)
                pe.wait_ge(h_hi_ready, HSPL * n + 2 * c + 2)
                pe.wait_ge(h_lo_ready, HSPL * n + 2 * c + 2)
                for j in range(J):
                    if c == 0:
                        pe.wait_ge(h_init, 4 * n + j + 1)
                    else:
                        pe.wait_ge(z_ready, SLOT * n + 2 * (c - 1) + j + 1)
                    weighted(ps_z[j], U3, j, h_hi[s], h_lo[s], True, True).then_inc(hu_done, 1)
                pe.wait_ge(a_hi_ready, ADJ * n + 2 * (2 + c) + 2)
                pe.wait_ge(a_lo_ready, ADJ * n + 2 * (2 + c) + 2)
                for j in range(J):
                    if c == 1:
                        pe.wait_ge(h_init, 4 * n + 2 * c + j + 1)
                    elif c > 1:
                        pe.wait_ge(nat_lo_ready, NAT * n + 2 * (c + 2) + j + 1)
                    weighted(ps_r[j], W4, j, a_hi[s], a_lo[s], True, True).then_inc(r_done, 1)
                for j in range(J):
                    pe.wait_ge(hu_copied, SLOT * n + 2 * c + j + 1)
                    weighted(ps_z[j], W3, j, a_hi[s], a_lo[s], False, True).then_inc(z_done, 1)
                if c == SLOTS - 1 and not last:
                    mixed(n + 1, 0, 0)
                for j in range(J):
                    if c == 0:
                        pe.wait_ge(x2_ready, 4 * n + 2 + j + 1)
                    else:
                        pe.wait_ge(v_ready, SLOT * n + 2 * (c - 1) + j + 1)
                    weighted(ps_v[j], W5, j, a_hi[s], a_lo[s], True, False)
                if c == 0:
                    turn_first(n, 1)
                else:
                    turn_back(n, c - 1)
                pe.wait_ge(rh_hi_ready, SLOT * n + 2 * c + 2)
                pe.wait_ge(rh_lo_ready, SLOT * n + 2 * c + 2)
                for j in range(J):
                    weighted(ps_v[j], U5, j, rh_hi, rh_lo, False, True).then_inc(v_done, 1)

            pe.wait_ge(ident_ready, 1)
            for c in range(T):
                turn_adj(c)
            for _ in range(WARM_TURNS):
                pe.transpose(ps_z[0][:, 0:P], ident[:], ident[:])
            mixed(0, 0, 0)
            for m in range(4):
                turn_weight(m)
            pe.wait_ge(setup_lo, SPLIT_W0 + 1)
            project(0, 0)
            turn_weight(4)
            pe.wait_ge(gate_sums_ready, 4)
            pe.wait_ge(setup_lo, SPLIT_W0 + 3)
            pe.transpose(ps_v[1][:, 0:3 * J], bias_sum[:], ident[0:3 * J, 0:3 * J]).then_inc(bias_turned, 1)
            mixed(0, 1, 1)
            pe.wait_ge(setup_lo, SPLITS)
            pe.wait_ge(gate_bias_ready, 1)

            def pair(n, last):
                turn_first(n, 0)
                project(n, 1)
                for c in range(SLOTS):
                    slot(n, c, last)
                if not last:
                    project(n + 1, 0)
                    mixed(n + 1, 1, 1)
                turn_back(n, SLOTS - 1)

            with pe.Fori(0, LAST) as n:
                pair(n, False)
            pair(LAST, True)

        @block.scalar
        def _(act):
            def split_adj(c):
                act.wait_ge(setup_turned, c + 1)
                act.activation(adjt_hi[:, :, c * P:(c + 1) * P], adj_bank[c][:].rearrange("p (g f) -> p g f", f=P),
                               ACT.Copy).then_inc(setup_hi, 1)

            def split_weight(m):
                act.wait_ge(setup_turned, T + m + 1)
                act.activation(w_hi[:, turned_weight[m]], weight_bank[m][:].rearrange("p (k o) -> p k o", k=J),
                               ACT.Copy).then_inc(setup_hi, 1)

            def split_norm(n, k):
                s = k % 2
                for b in range(J):
                    rows = slice(b * HALF, (b + 1) * HALF)
                    act.wait_ge(xn_ready, 2 * (LN * n + k) + b + 1)
                    act.activation(nat_hi[s][:, rows, :], xn[s][:, rows, :], ACT.Relu).then_inc(nat_hi_ready, 1)

            def split_mixed(n, q, s, tiles=range(J)):
                for j in tiles:
                    act.wait_ge(adj_done, ADJ * n + 2 * q + j + 1)
                    act.activation(a_hi[s][:, j, :], ps_a[j][:], ACT.Copy).then_inc(a_hi_ready, 1)

            def first_state(n, s):
                for j in range(J):
                    act.wait_ge(turned, TURN * n + 2 * s + j + 1)
                    act.activation(h[s][:, j, :], first_bank[s][j][:], ACT.Relu).then_inc(h_init, 1)
                for j in range(J):
                    act.wait_ge(h_init, 4 * n + 2 * s + j + 1)
                    act.activation(h_hi[s][:, j, :], h[s][:, j, :], ACT.Copy).then_inc(h_hi_ready, 1)

            def turned_state(n, c):
                s = c % 2
                for b in range(J):
                    act.wait_ge(turned, TURN * n + 2 * (c + 2) + b + 1)
                    act.activation(nat_hi[s][:, b * HALF:(b + 1) * HALF, :],
                                   ps_r[b][:].rearrange("p (t d) -> p t d", d=D), ACT.Copy).then_inc(nat_hi_ready, 1)

            def slot(n, c, last):
                s = c % 2
                split_mixed(n, 2 + c, s)
                if c == 0:
                    split_norm(n, 3)
                if c == SLOTS - 1 and not last:
                    split_norm(n + 1, 0)
                for j in range(J):
                    act.wait_ge(hu_done, SLOT * n + 2 * c + j + 1)
                    act.activation(hu[:, j, :], ps_z[j][:], ACT.Copy).then_inc(hu_copied, 1)
                for j in range(J):
                    act.wait_ge(r_sum_ready, SLOT * n + 2 * c + j + 1)
                    act.activation(r[:, j, :], r[:, j, :], ACT.Sigmoid,
                                   bias=gate_bias[:, 1, j:j + 1]).then_inc(r_ready, 1)
                for j in range(J):
                    act.wait_ge(rh_ready, SLOT * n + 2 * c + j + 1)
                    act.activation(rh_hi[:, j, :], r[:, j, :], ACT.Copy).then_inc(rh_hi_ready, 1)
                for j in range(J):
                    act.wait_ge(z_done, SLOT * n + 2 * c + j + 1)
                    act.activation(z[:, j, :], ps_z[j][:], ACT.Sigmoid,
                                   bias=gate_bias[:, 0, j:j + 1]).then_inc(z_ready, 1)
                if c == SLOTS - 1 and not last:
                    split_mixed(n + 1, 0, 0)
                    split_norm(n + 1, 1)
                if c == 0:
                    first_state(n, 1)
                elif c < SLOTS - 1:
                    turned_state(n, c - 1)
                for j in range(J):
                    act.wait_ge(v_done, SLOT * n + 2 * c + j + 1)
                    act.activation(v[:, j, :], ps_v[j][:], ACT.Tanh,
                                   bias=gate_bias[:, 2, j:j + 1]).then_inc(v_ready, 1)
                if c < SLOTS - 2:
                    for j in range(J):
                        act.wait_ge(h_new, SLOT * n + 2 * c + j + 1)
                        act.activation(h_hi[s][:, j, :], h[s][:, j, :], ACT.Copy).then_inc(h_hi_ready, 1)

            act.wait_ge(ident_ready, 1)
            act.activation(table_probe[:], ident[:, 0:1], ACT.Sigmoid)
            split_adj(0)
            split_adj(1)
            split_adj(2)
            split_norm(0, 0)
            split_adj(3)
            act.wait_ge(w0_loaded, 16)
            act.activation(w_hi[:, W0], w0_raw[:], ACT.Copy).then_inc(setup_hi, 1)
            split_mixed(0, 0, 0, [0])
            split_norm(0, 1)
            split_mixed(0, 0, 0, [1])
            for m in range(len(turned_weight)):
                split_weight(m)
            act.wait_ge(bias_turned, 1)
            act.activation(gate_bias[:], ps_v[1][:, 0:3 * J].rearrange("p (m j) -> p m j", j=J),
                           ACT.Copy).then_inc(gate_bias_ready, 1)
            act.wait_ge(gate_bias_ready, 1)
            split_mixed(0, 1, 1)
            split_norm(0, 2)

            def pair(n, last):
                first_state(n, 0)
                for c in range(SLOTS):
                    slot(n, c, last)
                if not last:
                    split_mixed(n + 1, 1, 1)
                    split_norm(n + 1, 2)

            with act.Fori(0, LAST) as n:
                pair(n, False)
            pair(LAST, True)

        @block.vector
        def _(dve):
            def split_adj(c):
                dve.wait_ge(setup_hi, c + 1)
                cols = slice(c * P, (c + 1) * P)
                dve.tensor_tensor(adjt_lo[:, :, cols], adj_bank[c][:].rearrange("p (g f) -> p g f", f=P),
                                  adjt_hi[:, :, cols].bitcast(F32), ALU.subtract).then_inc(setup_lo, 1)

            def split_weight(m):
                w = turned_weight[m]
                dve.wait_ge(setup_hi, SPLIT_W0 + m + 2)
                dve.tensor_tensor(w_lo[:, w], weight_bank[m][:].rearrange("p (k o) -> p k o", k=J),
                                  w_hi[:, w].bitcast(F32), ALU.subtract).then_inc(setup_lo, 1)

            def norm_stats(n, k, src):
                for t in range(T):
                    dve.bn_stats(stats[:, t, :], src[:, t, :])
                dve.drain()
                for t in range(T):
                    ins = dve.bn_aggr(meanvar[:, t, :], stats[:, t, :])
                ins.then_inc(var_ready, 1)
                dve.wait_ge(var_ready, LN * n + k + 1)
                dve.tensor_scalar(vareps[:], meanvar[:, :, 1], EPS, None, ALU.add).then_inc(vareps_ready, 1)

            def norm_rows(n, k, src):
                s = k % 2
                dve.wait_ge(rstd_ready, LN * n + k + 1)
                for t in range(T):
                    ins = dve.tensor_scalar(xn[s][:, t, :], src[:, t, :], meanvar[:, t, 0:1], rstd[:, t:t + 1],
                                            ALU.subtract, ALU.mult)
                    if t % HALF == HALF - 1:
                        ins.then_inc(xn_ready, 1)

            def norm_split(n, k):
                s = k % 2
                for b in range(J):
                    rows = slice(b * HALF, (b + 1) * HALF)
                    dve.wait_ge(nat_hi_ready, NAT * n + 2 * k + b + 1)
                    dve.scalar_tensor_tensor(out=nat_lo[s][:, rows, :], in0=xn[s][:, rows, :], scalar=0.0,
                                             in1=nat_hi[s][:, rows, :].bitcast(F32), op0=ALU.max,
                                             op1=ALU.subtract).then_inc(nat_lo_ready, 1)

            def first_stats(n, s):
                dve.wait_ge(x_loaded[s], 16 * n + 16)
                norm_stats(n, s, xs[s])

            def split_mixed(n, q, s, tiles=range(J)):
                for j in tiles:
                    dve.wait_ge(a_hi_ready, ADJ * n + 2 * q + j + 1)
                    dve.tensor_tensor(a_lo[s][:, j, :], ps_a[j][:], a_hi[s][:, j, :].bitcast(F32),
                                      ALU.subtract).then_inc(a_lo_ready, 1)

            def residual(n, s):
                dve.wait_ge(xb_ready, 2 * n + s + 1)
                bank = (ps_z, ps_v)[s]
                for b in range(J):
                    rows = slice(b * HALF, (b + 1) * HALF)
                    dve.wait_ge(proj_done, 4 * n + 2 * s + b + 1)
                    dve.tensor_tensor(x2[s][:, rows, :], bank[b][:].rearrange("p (t d) -> p t d", d=D),
                                      xs[s][:, rows, :], ALU.add).then_inc(x2_ready, 1)
                dve.wait_ge(x2_ready, 4 * n + 2 * s + 2)
                norm_stats(n, 2 + s, x2[s])

            def split_state(n, s, q):
                for j in range(J):
                    dve.wait_ge(h_hi_ready, HSPL * n + 2 * q + j + 1)
                    dve.tensor_tensor(h_lo[s][:, j, :], h[s][:, j, :], h_hi[s][:, j, :].bitcast(F32),
                                      ALU.subtract).then_inc(h_lo_ready, 1)

            def turned_state(n, c):
                s = c % 2
                for b in range(J):
                    rows = slice(b * HALF, (b + 1) * HALF)
                    dve.wait_ge(nat_hi_ready, NAT * n + 2 * (c + 4) + b + 1)
                    dve.tensor_tensor(nat_lo[s][:, rows, :], ps_r[b][:].rearrange("p (t d) -> p t d", d=D),
                                      nat_hi[s][:, rows, :].bitcast(F32), ALU.subtract).then_inc(nat_lo_ready, 1)

            def output(n, s):
                if isinstance(n, int) and n > 0:
                    dve.wait_ge(out_stored[s], 16 * J * n)
                for b in range(J):
                    rows = slice(b * HALF, (b + 1) * HALF)
                    dve.wait_ge(turned, TURN * n + 2 * (SLOTS + s) + b + 1)
                    dve.tensor_tensor(outs[s][:, rows, :], ps_r[b][:].rearrange("p (t d) -> p t d", d=D),
                                      x2[s][:, rows, :], ALU.add).then_inc(out_ready, 1)

            def slot(n, c, last):
                s = c % 2
                if c == 0:
                    split_mixed(n, 2 + c, s, [0])
                    norm_rows(n, 3, x2[1])
                    split_mixed(n, 2 + c, s, [1])
                    norm_split(n, 3)
                else:
                    split_mixed(n, 2 + c, s)
                if c == SLOTS - 1 and not last:
                    norm_rows(n + 1, 0, xs[0])
                    norm_split(n + 1, 0)
                for j in range(J):
                    dve.wait_ge(hu_copied, SLOT * n + 2 * c + j + 1)
                    dve.wait_ge(r_done, SLOT * n + 2 * c + j + 1)
                    dve.tensor_tensor(r[:, j, :], ps_r[j][:], hu[:, j, :], ALU.add).then_inc(r_sum_ready, 1)
                for j in range(J):
                    dve.wait_ge(r_ready, SLOT * n + 2 * c + j + 1)
                    dve.tensor_tensor(r[:, j, :], r[:, j, :], h[s][:, j, :], ALU.mult).then_inc(rh_ready, 1)
                for j in range(J):
                    dve.wait_ge(rh_hi_ready, SLOT * n + 2 * c + j + 1)
                    dve.tensor_tensor(rh_lo[:, j, :], r[:, j, :], rh_hi[:, j, :].bitcast(F32),
                                      ALU.subtract).then_inc(rh_lo_ready, 1)
                for j in range(J):
                    dve.wait_ge(z_ready, SLOT * n + 2 * c + j + 1)
                    dve.scalar_tensor_tensor(out=keep[:, j, :], in0=z[:, j, :], scalar=1.0, in1=h[s][:, j, :],
                                             op0=ALU.subtract, op1=ALU.mult).then_inc(keep_ready, 1)
                if c == SLOTS - 2 and not last:
                    first_stats(n + 1, 0)
                if c == SLOTS - 1 and not last:
                    first_stats(n + 1, 1)
                    split_mixed(n + 1, 0, 0)
                    norm_rows(n + 1, 1, xs[1])
                    norm_split(n + 1, 1)
                if c == 0:
                    split_state(n, 1, 1)
                elif c < SLOTS - 1:
                    turned_state(n, c - 1)
                else:
                    output(n, 0)
                for j in range(J):
                    dve.wait_ge(v_ready, SLOT * n + 2 * c + j + 1)
                    dve.tensor_tensor(v[:, j, :], v[:, j, :], z[:, j, :], ALU.mult).then_inc(zv_ready, 1)
                    dve.wait_ge(zv_ready, SLOT * n + 2 * c + j + 1)
                    dve.wait_ge(keep_ready, SLOT * n + 2 * c + j + 1)
                    dve.tensor_tensor(h[s][:, j, :], v[:, j, :], keep[:, j, :], ALU.subtract).then_inc(h_new, 1)
                if c < SLOTS - 2:
                    split_state(n, s, c + 2)

            def second_norm(n):
                split_mixed(n, 1, 1, [0])
                norm_rows(n, 2, x2[0])
                split_mixed(n, 1, 1, [1])
                norm_split(n, 2)

            first_stats(0, 0)
            split_adj(0)
            norm_rows(0, 0, xs[0])
            split_adj(1)
            norm_split(0, 0)
            split_adj(2)
            split_adj(3)
            dve.wait_ge(setup_hi, SPLIT_W0 + 1)
            dve.tensor_tensor(w_lo[:, W0], w0_raw[:], w_hi[:, W0].bitcast(F32), ALU.subtract).then_inc(setup_lo, 1)
            first_stats(0, 1)
            norm_rows(0, 1, xs[1])
            split_mixed(0, 0, 0)
            norm_split(0, 1)
            for m in range(4):
                split_weight(m)
            residual(0, 0)
            split_weight(4)
            second_norm(0)

            def pair(n, last):
                split_state(n, 0, 0)
                residual(n, 1)
                for c in range(SLOTS):
                    slot(n, c, last)
                if not last:
                    residual(n + 1, 0)
                    second_norm(n + 1)
                output(n, 1)
                dve.wait_ge(out_ready, 4 * n + 4)

            with dve.Fori(0, LAST) as n:
                pair(n, False)
            pair(LAST, True)


_INS = ["x", "adj", "L0_gnn_weight", "L0_gnn_bias", "L1_gnn_w3_w", "L1_gnn_w3_b", "L1_gnn_u3_w", "L1_gnn_u3_b",
        "L1_gnn_w4_w", "L1_gnn_w4_b", "L1_gnn_w5_w", "L1_gnn_w5_b", "L1_gnn_u5_w", "L1_gnn_u5_b"]


def kernel(**inputs):
    import numpy as _np
    import concourse.bacc as _bacc
    from concourse import mybir as _mybir
    from concourse.bass_utils import run_bass_kernel_spmd as _run

    nc = _bacc.Bacc("TRN2", target_bir_lowering=False, num_devices=1)
    arrays, args = {}, []
    for name in _INS:
        a = _np.ascontiguousarray(inputs[name])
        arrays[f"in_{name}_dram"] = a
        args.append(nc.dram_tensor(f"in_{name}_dram", a.shape, _mybir.dt.from_np(a.dtype), kind="ExternalInput").ap())
    shape = inputs["x"].shape
    args.append(nc.dram_tensor("out_0_dram", shape, _mybir.dt.float32, kind="ExternalOutput").ap())
    adjacency_blocks_kernel(nc, *args)
    result = _run(nc, [arrays], core_ids=[0])
    return result.results[0]["out_0_dram"]
```
